# Optimizing a Trainium2 kernel written in Bass

```python
import numpy as np
import jax
import jax.numpy as jnp

def _softmax(x, axis=-1):
    return jax.nn.softmax(x, axis=axis)

def _gelu(x):
    return jax.nn.gelu(x, approximate=True)

def _silu(x):
    return jax.nn.silu(x)

def _sigmoid(x):
    return jax.nn.sigmoid(x)

def _layernorm(x, axis=-1, eps=1e-05):
    m = jnp.mean(x, axis=axis, keepdims=True)
    v = jnp.var(x, axis=axis, keepdims=True)
    return (x - m) / jnp.sqrt(v + eps)

def _scatter_add(tgt, idx, src, axis=0):
    return tgt.at[idx].add(src)

def _segment_sum(src, seg, n):
    return jax.ops.segment_sum(src, seg, n)
kernel_name = 'mk_flamingo_gated_d2_seqx_r8_9332f6'

def setup_inputs(seed: int=0):
    np.random.seed(seed)
    _w = jnp.asarray

    def _rec_inputs():
        import jax
        import jax.numpy as jnp
        _rk = jax.random.key(seed)
        x = -0.0002928 + 1 * jax.random.normal(jax.random.fold_in(_rk, 1), (16, 128, 128), jnp.float32)
        _lenS = 128 - jax.random.randint(jax.random.fold_in(_rk, 7), (16,), 0, max(1, 128 // 4) + 1, jnp.int32)
        _lenS2 = 77 - jax.random.randint(jax.random.fold_in(_rk, 8), (16,), 0, max(1, 77 // 4) + 1, jnp.int32)
        _ctx_512P = jax.random.normal(jax.random.fold_in(_rk, 11), (16, 16, 64), jnp.float32)
        _ctx_512c = jax.random.dirichlet(jax.random.fold_in(_rk, 511), 0.3 * jnp.ones((16,), jnp.float32), (16, 77))
        _ctx_512t = jnp.einsum('bsk,bkd->bsd', _ctx_512c, _ctx_512P)
        _ctx_512t = _ctx_512t * jax.lax.rsqrt(jnp.mean(jnp.square(_ctx_512t)) + 1e-12) * 0.953939
        ctx_512 = -0.000514642 + 1.00011 * (_ctx_512t + 0.3 * jax.random.normal(jax.random.fold_in(_rk, 611), (16, 77, 64), jnp.float32))
        _g = jax.random.normal(jax.random.fold_in(_rk, 9001), (2, 2), jnp.float32)
        _g = jnp.sign(_g) * jnp.maximum(jnp.abs(_g), 1.0) + (_g == 0) * 1.0
        g_xattn = _g[0]
        g_ffn = _g[1]
        return (x, ctx_512, g_xattn, g_ffn)
    x, ctx_512, g_xattn, g_ffn = _rec_inputs()

    def _L0_xattn_setup():
        import jax, jax.numpy as jnp
        import numpy as np
        DIM = 128
        LATENT_DIM = 64
        NUM_HEADS = 16
        HEAD_DIM = DIM // NUM_HEADS
        SCALE = HEAD_DIM ** (-0.5)
        key = jax.random.key(seed)
        k1, k2, k3, k4, k5 = jax.random.split(key, 5)
        B, xN, zN = (2, 256, 256)
        x = jax.random.normal(k1, (B, xN, DIM), dtype=jnp.float32)
        z = jax.random.normal(k2, (B, zN, LATENT_DIM), dtype=jnp.float32)
        Wq = jax.random.normal(k3, (DIM, DIM), dtype=jnp.float32) * DIM ** (-0.5)
        Wkv = jax.random.normal(k4, (2 * DIM, LATENT_DIM), dtype=jnp.float32) * LATENT_DIM ** (-0.5)
        Wo = jax.random.normal(k5, (DIM, DIM), dtype=jnp.float32) * DIM ** (-0.5)
        return {'x': x, 'z': z, 'Wq': Wq, 'Wkv': Wkv, 'Wo': Wo}
    _L0_xattn_all = _L0_xattn_setup()
    _L0_xattn_in = {k: v for k, v in _L0_xattn_all.items() if k in ('Wq', 'Wkv', 'Wo')}
    del _L0_xattn_all

    def _L0_ffn_setup():
        import jax, jax.numpy as jnp
        import numpy as np
        TOP_K = 2
        key = jax.random.key(seed)
        k1, k2, k3, k4 = jax.random.split(key, 4)
        B, N, D, E, F = (4, 256, 128, 8, 512)
        x = jax.random.normal(k1, (B, N, D), dtype=jnp.float32)
        gate_w = jax.random.normal(k2, (D, E), dtype=jnp.float32) * D ** (-0.5)
        w1 = jax.random.normal(k3, (E, D, F), dtype=jnp.float32) * D ** (-0.5)
        w2 = jax.random.normal(k4, (E, F, D), dtype=jnp.float32) * F ** (-0.5)
        return {'x': x, 'gate_w': gate_w, 'w1': w1, 'w2': w2}
    _L0_ffn_all = _L0_ffn_setup()
    _L0_ffn_in = {k: v for k, v in _L0_ffn_all.items() if k in ('gate_w', 'w1', 'w2')}
    del _L0_ffn_all

    def _L1_xattn_setup():
        import jax, jax.numpy as jnp
        import numpy as np
        HEADS = 16
        D_MODEL = 128
        IMG_MODEL = 64
        D_K = D_MODEL // HEADS
        key = jax.random.key(seed)
        ks = jax.random.split(key, 12)
        B, LQ, LKV = (8, 256, 128)
        s_dm = 1.0 / np.sqrt(D_MODEL)
        s_im = 1.0 / np.sqrt(IMG_MODEL)
        return {'q': jax.random.normal(ks[0], (B, LQ, D_MODEL), jnp.float32), 'k': jax.random.normal(ks[1], (B, LKV, IMG_MODEL), jnp.float32), 'v': jax.random.normal(ks[2], (B, LKV, IMG_MODEL), jnp.float32), 'Wq': jax.random.normal(ks[3], (D_MODEL, D_MODEL), jnp.float32) * s_dm, 'bq': jnp.zeros((D_MODEL,), jnp.float32), 'Wk': jax.random.normal(ks[4], (IMG_MODEL, D_MODEL), jnp.float32) * s_im, 'bk': jnp.zeros((D_MODEL,), jnp.float32), 'Wv': jax.random.normal(ks[5], (IMG_MODEL, D_MODEL), jnp.float32) * s_im, 'bv': jnp.zeros((D_MODEL,), jnp.float32), 'Wo': jax.random.normal(ks[6], (D_MODEL, D_MODEL), jnp.float32) * s_dm, 'bo': jnp.zeros((D_MODEL,), jnp.float32)}
    _L1_xattn_all = _L1_xattn_setup()
    _L1_xattn_in = {k: v for k, v in _L1_xattn_all.items() if k in ('Wq', 'bq', 'Wk', 'bk', 'Wv', 'bv', 'Wo', 'bo')}
    del _L1_xattn_all

    def _L1_ffn_setup():
        import jax, jax.numpy as jnp
        import numpy as np
        B, S, D, F, E = (2, 256, 128, 512, 8)
        LN_EPS = 1e-05

        def _layer_norm(x, gamma, beta):
            mu = jnp.mean(x, axis=-1, keepdims=True)
            var = jnp.mean(jnp.square(x - mu), axis=-1, keepdims=True)
            return (x - mu) * jax.lax.rsqrt(var + LN_EPS) * gamma + beta
        key = jax.random.key(seed)
        ks = jax.random.split(key, 8)

        def xavier(k, shape):
            fan_in, fan_out = (shape[-1], shape[-2])
            a = jnp.sqrt(6.0 / (fan_in + fan_out))
            return jax.random.uniform(k, shape, jnp.float32, -a, a)
        return {'tgt': jax.random.normal(ks[0], (B, S, D), jnp.float32), 'Wr': xavier(ks[1], (E, D)), 'br': jnp.zeros((E,), jnp.float32), 'W1': xavier(ks[2], (E, F, D)), 'b1': jnp.zeros((E, F), jnp.float32), 'W2': xavier(ks[3], (E, D, F)), 'b2': jnp.zeros((E, D), jnp.float32), 'gamma': jnp.ones((D,), jnp.float32), 'beta': jnp.zeros((D,), jnp.float32)}
    _L1_ffn_all = _L1_ffn_setup()
    _L1_ffn_in = {k: v for k, v in _L1_ffn_all.items() if k in ('Wr', 'br', 'W1', 'b1', 'W2', 'b2', 'gamma', 'beta')}
    del _L1_ffn_all
    return {'x': x, 'ctx_512': ctx_512, 'g_xattn': g_xattn, 'g_ffn': g_ffn, 'L0_xattn_Wq': _L0_xattn_in['Wq'], 'L0_xattn_Wkv': _L0_xattn_in['Wkv'], 'L0_xattn_Wo': _L0_xattn_in['Wo'], 'L0_ffn_gate_w': _L0_ffn_in['gate_w'], 'L0_ffn_w1': _L0_ffn_in['w1'], 'L0_ffn_w2': _L0_ffn_in['w2'], 'L1_xattn_Wq': _L1_xattn_in['Wq'], 'L1_xattn_bq': _L1_xattn_in['bq'], 'L1_xattn_Wk': _L1_xattn_in['Wk'], 'L1_xattn_bk': _L1_xattn_in['bk'], 'L1_xattn_Wv': _L1_xattn_in['Wv'], 'L1_xattn_bv': _L1_xattn_in['bv'], 'L1_xattn_Wo': _L1_xattn_in['Wo'], 'L1_xattn_bo': _L1_xattn_in['bo'], 'L1_ffn_Wr': _L1_ffn_in['Wr'], 'L1_ffn_br': _L1_ffn_in['br'], 'L1_ffn_W1': _L1_ffn_in['W1'], 'L1_ffn_b1': _L1_ffn_in['b1'], 'L1_ffn_W2': _L1_ffn_in['W2'], 'L1_ffn_b2': _L1_ffn_in['b2'], 'L1_ffn_gamma': _L1_ffn_in['gamma'], 'L1_ffn_beta': _L1_ffn_in['beta']}

def reference(x, ctx_512, g_xattn, g_ffn, L0_xattn_Wq, L0_xattn_Wkv, L0_xattn_Wo, L0_ffn_gate_w, L0_ffn_w1, L0_ffn_w2, L1_xattn_Wq, L1_xattn_bq, L1_xattn_Wk, L1_xattn_bk, L1_xattn_Wv, L1_xattn_bv, L1_xattn_Wo, L1_xattn_bo, L1_ffn_Wr, L1_ffn_br, L1_ffn_W1, L1_ffn_b1, L1_ffn_W2, L1_ffn_b2, L1_ffn_gamma, L1_ffn_beta):
    import jax
    import jax.numpy as jnp

    def _L0_xattn_ref(x, z, Wq, Wkv, Wo):
        import jax, jax.numpy as jnp
        import numpy as np
        DIM = 128
        LATENT_DIM = 64
        NUM_HEADS = 16
        HEAD_DIM = DIM // NUM_HEADS
        SCALE = HEAD_DIM ** (-0.5)
        B, xN, _ = x.shape
        _, zN, _ = z.shape
        Q = (x @ Wq.T).reshape(B, xN, NUM_HEADS, HEAD_DIM)
        KV = (z @ Wkv.T).reshape(B, zN, 2, NUM_HEADS, HEAD_DIM)
        K = KV[:, :, 0]
        V = KV[:, :, 1]
        attn = jnp.einsum('bqhd,bkhd->bhqk', Q, K) * SCALE
        attn = jax.nn.softmax(attn, axis=-1)
        O = jnp.einsum('bhqk,bkhd->bqhd', attn, V).reshape(B, xN, DIM)
        return O @ Wo.T

    def _L0_ffn_ref(x, gate_w, w1, w2):
        import jax, jax.numpy as jnp
        import numpy as np
        TOP_K = 2
        E = gate_w.shape[-1]
        gate_logits = jnp.einsum('bnd,de->bne', x, gate_w)
        gate_probs = jax.nn.softmax(gate_logits, axis=-1)
        top_k_probs, top_k_idx = jax.lax.top_k(gate_probs, TOP_K)
        top_k_weights = top_k_probs / jnp.sum(top_k_probs, axis=-1, keepdims=True)
        comb = jnp.sum(jax.nn.one_hot(top_k_idx, E, dtype=x.dtype) * top_k_weights[..., None], axis=2)
        h = jax.nn.gelu(jnp.einsum('bnd,edf->benf', x, w1))
        expert_out = jnp.einsum('benf,efd->bend', h, w2)
        output = jnp.einsum('bne,bend->bnd', comb, expert_out)
        return output

    def _L1_xattn_ref(q, k, v, Wq, bq, Wk, bk, Wv, bv, Wo, bo):
        import jax, jax.numpy as jnp
        import numpy as np
        HEADS = 16
        D_MODEL = 128
        IMG_MODEL = 64
        D_K = D_MODEL // HEADS
        B, LQ, _ = q.shape
        LKV = k.shape[1]
        qh = (q @ Wq + bq).reshape(B, LQ, HEADS, D_K).transpose(0, 2, 1, 3)
        kh = (k @ Wk + bk).reshape(B, LKV, HEADS, D_K).transpose(0, 2, 1, 3)
        vh = (v @ Wv + bv).reshape(B, LKV, HEADS, D_K).transpose(0, 2, 1, 3)
        scale = 1.0 / np.sqrt(D_K)
        scores = jnp.einsum('bhqd,bhkd->bhqk', qh, kh) * scale
        attn = jax.nn.softmax(scores, axis=-1)
        out = jnp.einsum('bhqk,bhkd->bhqd', attn, vh)
        concat = out.transpose(0, 2, 1, 3).reshape(B, LQ, D_MODEL)
        return concat @ Wo + bo

    def _L1_ffn_ref(tgt, Wr, br, W1, b1, W2, b2, gamma, beta):
        import jax, jax.numpy as jnp
        import numpy as np
        B, S, D, F, E = (2, 256, 128, 512, 8)
        LN_EPS = 1e-05

        def _layer_norm(x, gamma, beta):
            mu = jnp.mean(x, axis=-1, keepdims=True)
            var = jnp.mean(jnp.square(x - mu), axis=-1, keepdims=True)
            return (x - mu) * jax.lax.rsqrt(var + LN_EPS) * gamma + beta
        logits = jnp.einsum('bsd,ed->bse', tgt, Wr) + br
        top_v, top_i = jax.lax.top_k(logits, 2)
        top_w = jax.nn.softmax(top_v, axis=-1)
        n_exp = logits.shape[-1]
        router_w = jnp.sum(jax.nn.one_hot(top_i, n_exp, dtype=top_w.dtype) * top_w[..., None], axis=-2)
        h = jnp.einsum('bsd,efd->bsef', tgt, W1) + b1
        h = jax.nn.relu(h)
        o = jnp.einsum('bsef,edf->bsed', h, W2) + b2
        tgt2 = jnp.einsum('bsed,bse->bsd', o, router_w)
        return _layer_norm(tgt + tgt2, gamma, beta)
    x = x + jnp.tanh(g_xattn[0]) * _L0_xattn_ref(_layernorm(x, axis=-1), ctx_512, L0_xattn_Wq, L0_xattn_Wkv, L0_xattn_Wo)
    x = x + jnp.tanh(g_ffn[0]) * _L0_ffn_ref(_layernorm(x, axis=-1), L0_ffn_gate_w, L0_ffn_w1, L0_ffn_w2)
    x = x + jnp.tanh(g_xattn[1]) * _L1_xattn_ref(_layernorm(x, axis=-1), ctx_512, ctx_512, L1_xattn_Wq, L1_xattn_bq, L1_xattn_Wk, L1_xattn_bk, L1_xattn_Wv, L1_xattn_bv, L1_xattn_Wo, L1_xattn_bo)
    x = x + jnp.tanh(g_ffn[1]) * _L1_ffn_ref(_layernorm(x, axis=-1), L1_ffn_Wr, L1_ffn_br, L1_ffn_W1, L1_ffn_b1, L1_ffn_W2, L1_ffn_b2, L1_ffn_gamma, L1_ffn_beta)
    return x

_drawn_inputs = setup_inputs


def setup_inputs(seed=0):
    import zlib

    import numpy as np

    out = dict(_drawn_inputs(seed))
    spreads = {'g_ffn': (-1.0, 0.2),
     'L1_xattn_bq': (0.0, 0.1),
     'L1_xattn_bk': (0.0, 0.1),
     'L1_xattn_bv': (0.0, 0.1),
     'L1_xattn_bo': (0.0, 0.1),
     'L1_ffn_br': (0.0, 0.1),
     'L1_ffn_b1': (0.0, 0.1),
     'L1_ffn_b2': (0.0, 0.1),
     'L1_ffn_gamma': (1.0, 0.2),
     'L1_ffn_beta': (0.0, 0.1)}
    factors = {}
    for name, (base, spread) in spreads.items():
        noise = np.random.default_rng([zlib.crc32(name.encode()), seed]).standard_normal(out[name].shape)
        drawn = base * np.exp(spread * noise) if base else spread * noise
        out[name] = jnp.asarray(drawn.astype(out[name].dtype))
    for name, factor in factors.items():
        out[name] = (out[name] * factor).astype(out[name].dtype)
    return out
```

```python
from contextlib import ExitStack

import concourse.bass as bass
from concourse import mybir

F32 = mybir.dt.float32
I32 = mybir.dt.int32
U32 = mybir.dt.uint32
BF16 = mybir.dt.bfloat16
ALU = mybir.AluOpType
ACT = mybir.ActivationFunctionType
AX = mybir.AxisListType

P = 128
B = 16
D = 128
T = 128
KL = 77
C = 64
H = 16
HD = D // H
E = 8
F = 512
FC = F // P
EPS = 1e-5
SCALE = HD ** -0.5
NTOK = B * T
NPAIR = 2 * NTOK
REGION = P + NTOK
ROW = D + 2
NT = 40
UN = 4
Q_PART = (0, 0, 0, 1, 1, 2)
K_PART = (0, 1, 2, 0, 1, 0)
NS = len(Q_PART)
MAXROW = NS * HD
KR = MAXROW + 2
SM_UNITS = ((0, 6), (6, 12), (12, 16))


class Step:

    def __init__(self, c, i=None):
        self.c, self.i = c, i

    def back(self, n):
        return Step(self.c - n, self.i)

    def at(self, mult, add=0):
        v = self.c * mult + add
        return v if self.i is None else self.i * (UN * mult) + v

    def lap(self, n, mult, add=0):
        v = (self.c // n) * mult + add
        return v if self.i is None else self.i * (UN // n * mult) + v

    def slot(self, n):
        return self.c % n


class Stage:

    def __init__(self, sem, n, every=1, base=0):
        self.sem, self.n, self.every, self.base = sem, n, every, base

    def wait(self, eng, b, k=None):
        v = b.lap(self.every, self.n, self.base + (self.n if k is None else k))
        if not isinstance(v, int) or v > self.base:
            eng.wait_ge(self.sem, v)


class Ring:

    def __init__(self, sems, per, laps=0):
        self.sems, self.per, self.laps = sems, per, laps

    def __getitem__(self, r):
        return self.sems[r]

    def wait(self, eng, b):
        v = b.lap(UN, self.per, self.per * (1 + self.laps))
        if not isinstance(v, int) or v > self.per * self.laps:
            eng.wait_ge(self.sems[b.slot(UN)], v)


def pipeline(eng, n, lead, deep, step):
    trips = (n - lead) // UN
    for s in range(lead):
        step(Step(s))
    with eng.Fori(0, trips) as i:
        for u in range(UN):
            step(Step(lead + u, i))
    for s in range(lead + trips * UN, n + deep):
        step(Step(s))


def build(nc, a, out):
    ctx = ExitStack()
    with ctx:
        def sb(name, shape, dt=F32):
            return ctx.enter_context(nc.sbuf_tensor(name, shape, dt))

        def sem(name):
            return ctx.enter_context(nc.semaphore(name))

        x = sb("x", [P, B * D])
        tgt = sb("tgt", [P, B * D])
        wa1 = sb("wa1", [P, E * F])
        wa2 = sb("wa2", [P, E * F])
        wb1 = sb("wb1", [P, E * F])
        wb2 = sb("wb2", [P, E * F])
        ctxT = sb("ctxT", [C, B * KL])
        room_k = sb("room_k", [KR, H * B * KL], BF16)
        k_all = room_k[:, :].rearrange("p (h k) -> p h k", h=H)
        room_q = sb("room_q", [P, UN * H * T], BF16)
        q_st = [room_q[0:KR, r * H * T:(r + 1) * H * T].rearrange("p (h q) -> p h q", h=H) for r in range(UN)]
        room = sb("room", [P, 5300])
        taken = {"attention": 0, "experts": 0}

        def part(user, p, n, dt=F32):
            words = n if dt == F32 else n // 2
            o = taken[user]
            taken[user] += words
            assert o + words <= 5300
            ap = room[0:p, o:o + words]
            return ap if dt == F32 else ap.bitcast(dt)

        k_st = [part("attention", KR, H * KL, BF16).rearrange("p (h k) -> p h k", h=H) for r in range(UN)]
        v_all = sb("v_all", [KL, B * D])
        ctx_nat = v_all[:, 0:B * C].rearrange("p (b c) -> p b c", b=B)
        v_x = [sb(f"v_x{r}", [KL, H, 32]) for r in range(2)]
        probs = [part("attention", KL, 4 * T).rearrange("p (i q) -> p i q", i=4) for r in range(4)]
        k_f = tgt[:, 0:B * KL]
        k_res = room_q[:, 0:2 * B * KL].bitcast(F32)
        k_p = room_q[:, 2 * B * KL:5 * B * KL].rearrange("p (s n) -> p s n", s=3)
        xn = [sb(f"xn{r}", [P, D]) for r in range(2)]
        xnT = sb("xnT", [P, T])
        q_f = sb("q_f", [P, T])
        q_res = sb("q_res", [P, T])
        q_p = [sb(f"q_p{r}", [P, 3, T], BF16) for r in range(2)]
        stats = [sb(f"stats{r}", [P, 6]) for r in range(2)]
        mv = [sb(f"mv{r}", [P, 2]) for r in range(2)]
        rstd = [sb(f"rstd{r}", [P, 2]) for r in range(2)]
        mx = [sb(f"mx{r}", [P, H]) for r in range(2)]
        mxp = [sb(f"mxp{r}", [P, 2, H], BF16) for r in range(2)]
        mxT = [sb(f"mxT{r}", [2 * H, T], BF16) for r in range(2)]
        od = part("attention", P, 2 * T)
        rec = part("attention", P, 2 * T)
        on = part("attention", P, 2 * T)
        fstats = sb("fstats", [P, 2, 6])
        fmv = sb("fmv", [P, 2, 2])
        frs = sb("frs", [P, 2, 2])
        xfp = [sb(f"xfp{r}", [P, 2, ROW]) for r in range(2)]
        xfT = sb("xfT", [P, 2 * T])
        lg = sb("lg", [P, 2, E])
        top = sb("top", [P, 2, 8])
        topi = sb("topi", [P, 2, 8], U32)
        ei = sb("ei", [P, 2, 2])
        oh = sb("oh", [P, 4, E])
        mb = sb("mb", [P, 2, E], BF16)
        cum = sb("cum", [P, E], BF16)
        gap = sb("gap", [P, 2])
        gexp = sb("gexp", [P, 2])
        gden = sb("gden", [P, 2])
        w0s = sb("w0s", [P, 2])
        w01 = sb("w01", [P, B * 2])
        w01g = sb("w01g", [P, B * 2])
        rk = sb("rk", [P, 2, E])
        pick = sb("pick", [P, 4, E])
        slots = [sb(f"slots{r}", [P, 4], I32) for r in range(2)]
        nE = sb("nE", [P, E])
        cmp16 = sb("cmp16", [P, E, B])
        tE = sb("tE", [P, E])
        cmp8 = sb("cmp8", [P, E, E])
        cE = sb("cE", [P, E])
        fE = sb("fE", [P, E])
        t8a = part("experts", P, NT * E).rearrange("p (t e) -> p t e", t=NT)
        t8b = part("experts", P, NT * E).rearrange("p (t e) -> p t e", t=NT)
        t_e = sb("t_e", [P, NT])
        t_n = sb("t_n", [P, NT])
        t_f = sb("t_f", [P, NT])
        t_j = sb("t_j", [P, NT])
        t_rel = sb("t_rel", [P, NT])
        t_valid = sb("t_valid", [P, NT])
        t_alt = sb("t_alt", [P, NT])
        t_ec = sb("t_ec", [P, NT])
        t_row = sb("t_row", [P, NT])
        r_row = sb("r_row", [P, NT], I32)
        r_exp = sb("r_exp", [P, NT], I32)
        xg = [part("experts", P, ROW) for r in range(UN)]
        xgT = [part("experts", P, P) for r in range(2)]
        hid = [part("experts", P, F) for r in range(2)]
        hidT = [part("experts", P, FC * P) for r in range(2)]
        o_sb = [part("experts", P, D) for r in range(UN)]
        idf = sb("idf", [P, 2])
        ids = [sb(f"ids{r}", [P, 1], I32) for r in range(UN)]
        ob = [sb(f"ob{r}", [P, 2, D]) for r in range(UN)]
        mix = [part("experts", P, D) for r in range(UN)]
        res = [part("experts", P, D) for r in range(UN)]
        ident = sb("ident", [P, P])
        identb = sb("identb", [P, P], BF16)
        tri = sb("tri", [P, P], BF16)
        onesb = sb("onesb", [P, P], BF16)
        negb = sb("negb", [P, 2 * H * B * KL // P], BF16)
        sel = sb("sel", [P, 2 * P])
        mhalf = sb("mhalf", [P, 2])
        iota8 = sb("iota8", [P, E])
        regoff = sb("regoff", [P, E])
        iota16 = sb("iota16", [P, B])
        iotat = sb("iotat", [P, NT])
        iotap = sb("iotap", [P, 1])
        tok = sb("tok", [P, B])
        altbase = sb("altbase", [P, NT])
        lt8 = sb("lt8", [P, E, E])
        zero_row = sb("zero_row", [P, ROW])
        g_in = sb("g_in", [P, 4])
        tg = sb("tg", [P, 4])
        gate = [sb(f"gate{l}", [P, E]) for l in range(2)]
        wq = [sb(f"wq{l}", [P, D]) for l in range(2)]
        wk = [sb(f"wk{l}", [C, D]) for l in range(2)]
        wv = [sb(f"wv{l}", [C, D]) for l in range(2)]
        wo = [sb(f"wo{l}", [P, 2 * D]) for l in range(2)]
        wo_perm = sb("wo_perm", [P, 2 * D])
        w_nat = sb("w_nat", [P, 4, D])
        wr_nat = sb("wr_nat", [E, D])
        wkv_nat = sb("wkv_nat", [P, 2, C])
        wk1_nat = sb("wk1_nat", [C, D])
        br = sb("br", [P, E])
        bo = sb("bo", [P, D])
        bv = sb("bv", [KL, D])
        bqk = sb("bqk", [P, 2])
        bqs = sb("bqs", [P, 1])
        gam = sb("gam", [P, D])
        bet = sb("bet", [P, D])
        b1_in = sb("b1_in", [32, P])
        b1_res = part("experts", 32, P)
        b1_p = sb("b1_p", [32, 3, P], BF16)
        b1r = room_k[0:3, 0:E * F]
        b2_in = sb("b2_in", [E, D])
        b2_res = part("experts", E, D)
        b2_p = sb("b2_p", [E, 3, D], BF16)
        b2r = room_k[0:3, E * F:2 * E * F]

        bank = [ctx.enter_context(nc.psum_tensor(f"bank{i}", [P, 512], F32)) for i in range(8)]
        xg_dram = nc.dram_tensor("xg_rows", [E * REGION, ROW], F32, kind="Internal").ap()
        o_dram = [nc.dram_tensor(f"o_rows{l}", [NPAIR + NT * P, D], F32, kind="Internal").ap() for l in range(2)]

        ld = {k: sem("ld_" + k) for k in
              ("x0", "x1", "x2", "x3", "ctx", "w0", "w1", "wa1", "wa2", "wb1", "wb2", "bias", "neg")}
        phase = sem("phase")
        const = sem("const")
        own = {e: sem("own_" + e) for e in ("pool", "dve", "act", "pe")}
        told = {k: sem("m_" + k) for k in
                ("neg", "ident", "tg", "ctxT", "ctxS", "free1", "v_raw1") + tuple(
                    f"{k}{l}" for l in range(2)
                    for k in ("wT", "w", "perm", "woT", "woS", "k", "v", "kparts", "count", "tiles"))}

        def tell(eng, name):
            eng.sem_inc(told[name], 1)

        def hear(eng, name):
            eng.wait_ge(told[name], 1)

        counts = {e: 0 for e in own}

        def linker(eng, name):
            def link(ins):
                counts[name] += 1
                ins.then_inc(own[name], 1)
                eng.wait_ge(own[name], counts[name])
            return link

        ONE = dict(xn=1, t1=1, c1=1, q=1, qs=2, qp=3, sm=3, mx=3, mp=2, mt=1, mtc=1, st=4, ex=4, pv=4, od=1,
                   bc=1, ro=2, wo=1, x2=1, vx=4, ln1=2, rs1=2, xb=1, cmb=2,
                   xt=1, xtc=1, id=3, m1=1, act=1, ht=1, htc=1, m2=1, oc=1)
        PAIR = dict(f1=4, rs2=2, f2=2, t2=1, c2=1, lg=1, f3=9, ew=1, rk=1, f4=10, xc=1)
        both = {k: sem(f"s_{k}") for k in ONE | PAIR}
        per_tile = ("xt", "xtc", "id", "m1", "act", "ht", "htc", "m2", "oc")
        layers = [
            {k: Stage(both[k], n, 1, l * n * (NT if k in per_tile else 0 if k in ("xb", "cmb") else B))
             for k, n in ONE.items()}
            | {k: Stage(both[k], n, 2, n + l * n * (0 if k == "xc" else B // 2)) for k, n in PAIR.items()}
            for l in range(2)]
        fa = Stage(sem("s_fa"), 3)
        fmvd = Stage(sem("s_fmv"), 1)
        frp = Stage(sem("s_frp"), 2)
        fb = Stage(sem("s_fb"), 3)

        def rings(name, per, laps):
            sems = [sem(f"{name}{r}") for r in range(UN)]
            return [Ring(sems, per, l * laps) for l in range(2)]

        s_qd = rings("s_qd", 16 * NS, B // UN)
        s_kd = rings("s_kd", 16, B // UN)
        s_md = rings("s_md", 16, B // UN)
        s_xg = rings("s_xg", 16, NT // UN)
        s_os = rings("s_os", 16, NT // UN)
        s_ob = rings("s_ob", 32, B // UN)
        s_store = rings("s_store", 16, 0)[0]
        s_kall = sem("s_kall")
        s_sc = [sem(f"s_sc{r}") for r in range(2)]
        SC_LAYER = 64 * B // 4

        block = ctx.enter_context(nc.Block())

        def end_phase(eng):
            eng.drain().then_inc(phase, 1)

        def apart(eng):
            eng.nop(nofuse=True)

        def seq(b):
            return bass.ds(b.at(D), D)

        def live(b):
            return b.i is not None or 0 <= b.c < B

        def live_pair(b):
            return b.c % 2 == 1 and live(b)


        LATE = [
            (w_nat[:, 2, :], a["L1_xattn_Wq"]), (w_nat[:, 3, :], a["L1_xattn_Wo"]),
            (wk1_nat[:, :], a["L1_xattn_Wk"]), (wv[1][:, :], a["L1_xattn_Wv"]), (wr_nat[:, :], a["L1_ffn_Wr"]),
            (br[:, :], a["L1_ffn_br"].partition_broadcast(P)), (bo[:, :], a["L1_xattn_bo"].partition_broadcast(P)),
            (bv[:, :], a["L1_xattn_bv"].partition_broadcast(KL)),
            (gam[:, :], a["L1_ffn_gamma"].partition_broadcast(P)),
            (bet[:, :], a["L1_ffn_beta"].partition_broadcast(P)),
            (b1_in[:, :], a["L1_ffn_b1"].rearrange("e (g n) -> (e g) n", n=P)), (b2_in[:, :], a["L1_ffn_b2"]),
        ] + [
            (bqk[:, j:j + 1], a[n].rearrange("(h d o) -> d h o", d=HD, o=1))
            for j, n in enumerate(("L1_xattn_bq", "L1_xattn_bk"))
        ]

        w_turned, w_copied = sem("w_turned"), sem("w_copied")

        def tile_live(t):
            return t.i is not None or 0 <= t.c < NT

        @block.sync
        def _(sp):
            def load(dst, src, key):
                sp.dma_start(dst, src).then_inc(ld[key], 16)

            load(ctx_nat[:, :, :], a["ctx_512"].rearrange("b k c -> k b c"), "ctx")
            load(wkv_nat[:, :, :], a["L0_xattn_Wkv"].rearrange("(s o) c -> o s c", s=2), "w0")
            load(w_nat[:, 0, :], a["L0_xattn_Wq"], "w0")
            load(w_nat[:, 1, :], a["L0_xattn_Wo"], "w0")
            load(g_in[:, 0:2], a["g_xattn"].partition_broadcast(P), "w0")
            load(g_in[:, 2:4], a["g_ffn"].partition_broadcast(P), "w0")
            load(gate[0][:, :], a["L0_ffn_gate_w"], "w0")
            for k in range(4):
                load(x[:, 4 * k * D:4 * (k + 1) * D].rearrange("p (b d) -> p b d", b=4),
                     a["x"][4 * k:4 * k + 4].rearrange("b p d -> p b d"), f"x{k}")

            def move_k(l):
                for s in range(NS):
                    sp.dma_start(k_all[HD * s:HD * (s + 1), :, :], k_p[:, K_PART[s], :]).then_inc(s_kall, 16)
                sp.wait_ge(s_kall, 16 * NS * (l + 1))

            hear(sp, "neg")
            load(k_all[MAXROW:KR, :, :], negb[:, :], "neg")
            hear(sp, "kparts0")
            move_k(0)
            sp.wait_ge(ld["neg"], 16)

            def load_rest():
                load(wa1[:, :].rearrange("p (e f) -> p e f", e=E), a["L0_ffn_w1"].rearrange("e d f -> d e f"), "wa1")
                load(wa2[:, :].rearrange("p (e c d) -> p e c d", e=E, c=FC),
                     a["L0_ffn_w2"].rearrange("e (c p) d -> p e c d", p=P), "wa2")
                with nc.allow_non_contiguous_dma(reason="two biases of 128 numbers, reordered"):
                    for dst, src in LATE:
                        load(dst, src, "w1")
                load(wb1[:, :].rearrange("p (e c d) -> p e c d", e=E, c=FC),
                     a["L1_ffn_W1"].rearrange("e (c p) d -> p e c d", p=P), "wb1")
                load(wb2[:, :].rearrange("p (e f) -> p e f", e=E), a["L1_ffn_W2"].rearrange("e d f -> d e f"), "wb2")

            def attention(l):
                S = layers[l]

                def step(s):
                    b = s.back(2)
                    if live(b):
                        S["st"].wait(sp, b.back(UN))
                        apart(sp)
                        sp.dma_start(k_st[b.slot(UN)][:, :, :], k_all[:, :, bass.ds(b.at(KL), KL)])\
                            .then_inc(s_kd[l][b.slot(UN)], 16)
                    if l == 1 and live(s):
                        S["cmb"].wait(sp, s.back(UN))
                        apart(sp)
                        for k in range(2):
                            sp.dma_start(ob[s.slot(UN)][:, k, :], o_dram[0][bass.ds(s.at(T, k * NTOK), T), :])\
                                .then_inc(s_ob[0][s.slot(UN)], 16)
                    b = s.back(3)
                    if live(b):
                        S["mtc"].wait(sp, b)
                        apart(sp)
                        sp.dma_start(q_st[b.slot(UN)][MAXROW:KR, :, :], mxT[b.slot(2)][:, :])\
                            .then_inc(s_md[l][b.slot(UN)], 16)
                    b = s.back(1)
                    if live(b):
                        S["st"].wait(sp, b.back(UN))
                        apart(sp)
                        S["qp"].wait(sp, b)
                        apart(sp)
                        for r in range(NS):
                            sp.dma_start(q_st[b.slot(UN)][HD * r:HD * (r + 1), :, :], q_p[b.slot(2)][:, Q_PART[r], :])\
                                .then_inc(s_qd[l][b.slot(UN)], 16)
                return step

            def load_tiles(l):
                S = layers[l]
                hear(sp, f"tiles{l}")
                for r in range(2):
                    sp.wait_ge(s_sc[r], 64 + SC_LAYER * (l + 1))
                if l == 1:
                    for i in range(3):
                        load(b1r[i:i + 1, :], b1_p[:, i, :], "bias")
                        load(b2r[i:i + 1, :].rearrange("p (e f) -> p e f", e=E)[:, :, 0:D], b2_p[:, i, :], "bias")
                row = sp.alloc_register(f"row{l}")

                def tile(t):
                    S["xt"].wait(sp, t.back(UN))
                    apart(sp)
                    S["id"].wait(sp, t.back(UN))
                    apart(sp)
                    sp.reg_load(row, r_row[0:1, bass.ds(t.at(1), 1)])
                    r = sp.snap(row, min_val=0, max_val=E * REGION - P)
                    sp.dma_start(xg[t.slot(UN)][:, :], xg_dram[bass.ds(r, P), :]).then_inc(s_xg[l][t.slot(UN)], 16)
                pipeline(sp, NT, UN, 0, tile)

            sp.wait_ge(phase, 4)
            load_rest()
            pipeline(sp, B, 8, 7, attention(0))
            load_tiles(0)
            hear(sp, "kparts1")
            move_k(1)
            sp.wait_ge(phase, 12)
            pipeline(sp, B, 8, 7, attention(1))
            load_tiles(1)
            sp.wait_ge(phase, 20)

            def last(s):
                b = s.back(3)
                if live(b):
                    fb.wait(sp, b)
                    apart(sp)
                    sp.dma_start(out[bass.ds(b.at(1), 1), :, :].rearrange("a p d -> p (a d)") if b.i is not None
                                 else out[b.c], res[b.slot(UN)][:, :]).then_inc(s_store[b.slot(UN)], 16)
                if live(s):
                    fa.wait(sp, s.back(UN))
                    apart(sp)
                    for k in range(2):
                        sp.dma_start(ob[s.slot(UN)][:, k, :], o_dram[1][bass.ds(s.at(T, k * NTOK), T), :])\
                            .then_inc(s_ob[1][s.slot(UN)], 16)
            pipeline(sp, B, 8, 3, last)
            for r in range(UN):
                sp.wait_ge(s_store[r], 16 * B // UN)


        @block.gpsimd
        def _(pool):
            link = linker(pool, "pool")

            def fill(out_, pattern, base, mult, keep=ALU.not_equal, value=1.0):
                link(pool.affine_select(out=out_, in_=out_, compare_op=keep, fill=value, base=base,
                                        pattern=pattern, channel_multiplier=mult))

            def iota(out_, pattern, base, mult):
                pool.iota(out_, pattern=pattern, base=base, channel_multiplier=mult,
                          allow_small_or_imprecise_dtypes=True).then_inc(own["pool"], 1)
                counts["pool"] += 1

            for k, n in PAIR.items():
                pool.sem_inc(both[k], n)
            link(pool.memset(ident[:, :], 0.0))
            fill(ident[:, :], [[-1, P]], 0, 1)
            link(pool.tensor_copy(identb[:, :], ident[:, :]))
            link(pool.memset(negb[:, :], -1.0))
            tell(pool, "neg")
            tell(pool, "ident")
            link(pool.memset(sel[:, :], 0.0))
            s0 = sel[:, 0:P].rearrange("p (i j d) -> p i j d", i=4, j=4)
            fill(s0[:, :, 0:3, :], [[-32, 4], [-1, 3], [0, HD]], -24, 1)
            fill(s0[:, :, 3, :], [[-32, 4], [0, HD]], -24, 1)
            fill(sel[:, P:2 * P].rearrange("p (i r) -> p i r", i=4), [[-32, 4], [0, 32]], -24, 1)
            link(pool.memset(tri[:, :], 1.0))
            fill(tri[:, :], [[1, P]], 0, -1, ALU.is_gt, 0.0)
            link(pool.memset(onesb[:, :], 1.0))
            link(pool.memset(mhalf[:, :], -0.5))
            link(pool.memset(zero_row[:, :], 0.0))
            for e in range(E):
                pool.dma_start(xg_dram[e * REGION:e * REGION + P, :], zero_row[:, :]).then_inc(s_sc[e % 2], 16)
            link(pool.memset(lt8[:, :, :], 1.0))
            fill(lt8[:, :, :], [[1, E], [-1, E]], 0, 0, ALU.is_ge, 0.0)
            iota(iota8[:, :], [[1, E]], 0, 0)
            iota(regoff[:, :], [[REGION, E]], P, 0)
            iota(iota16[:, :], [[P, B]], 0, 0)
            iota(iotat[:, :], [[1, NT]], 0, 0)
            iota(iotap[:, :], [[0, 1]], 0, 1)
            iota(tok[:, :], [[T, B]], 0, 1)
            iota(altbase[:, :], [[P, NT]], NPAIR, 1)
            for r in range(2):
                link(pool.memset(v_x[r][:, :, :], 0.0))
                for u in range(4):
                    link(pool.memset(v_x[r][:, 4 * u:4 * u + 4, 24 + u % 3:25 + u % 3], 1.0))
            pool.wait_ge(own["pool"], counts["pool"])
            end_phase(pool)
            pool.wait_ge(phase, 4)

            def rsqrt(stage_, b, out_, tmp, var, exp_):
                apart(pool)
                pool.tensor_scalar(tmp, var, EPS, None, ALU.add).then_inc(stage_.sem, 1)
                stage_.wait(pool, b, 1)
                pool.tensor_tensor(out_, tmp, exp_, ALU.pow).then_inc(stage_.sem, 1)

            def attention(l):
                S = layers[l]

                def step(s):
                    b = s.back(3)
                    if live(b):
                        S["pv"].wait(pool, b.back(2))
                        for u in range(4):
                            c0 = HD * (u % 3)
                            pool.tensor_copy(v_x[b.slot(2)][:, 4 * u:4 * u + 4, c0:c0 + HD],
                                             v_all[:, bass.ds(b.at(D, 4 * HD * u), 4 * HD)]
                                             .rearrange("p (i d) -> p i d", i=4)).then_inc(S["vx"].sem, 1)
                    if l == 1:
                        b = s.back(2)
                        if live(b):
                            S["xn"].wait(pool, b)
                            pool.tensor_tensor(x[:, seq(b)], x[:, seq(b)], bo[:, :], ALU.add).then_inc(S["xb"].sem, 1)
                    b = s.back(6)
                    if live_pair(b):
                        S["f1"].wait(pool, b)
                        rsqrt(S["rs2"], b, frs[:, :, 1], frs[:, :, 0], fmv[:, :, 1], mhalf[:, :])
                    if live(s):
                        S["ln1"].wait(pool, s)
                        rsqrt(S["rs1"], s, rstd[s.slot(2)][:, 1:2], rstd[s.slot(2)][:, 0:1], mv[s.slot(2)][:, 1:2],
                              mhalf[:, 0:1])
                    b = s.back(8)
                    if live_pair(b):
                        r = b.c // 2 % 2
                        if l == 1:
                            S["f2"].wait(pool, b)
                            pool.tensor_copy(tgt[:, bass.ds(b.at(D, -D), 2 * D)].rearrange("p (j d) -> p j d", j=2),
                                             xfp[r][:, :, 0:D]).then_inc(S["xc"].sem, 1)
                        S["f4"].wait(pool, b, 5)
                        apart(pool)
                        for j in range(2):
                            for k in range(2):
                                pool.indirect_dma_start(
                                    out=xg_dram, in_=xfp[r][:, j, :], in_offset=None,
                                    out_offset=bass.IndirectOffsetOnAxis(ap=slots[r][:, 2 * j + k:2 * j + k + 1], axis=0),
                                ).then_inc(s_sc[r], 16)
                return step

            def scatter_tiles(l):
                S = layers[l]

                def tile(t):
                    S["oc"].wait(pool, t)
                    S["id"].wait(pool, t)
                    apart(pool)
                    pool.indirect_dma_start(
                        out=o_dram[l], in_=o_sb[t.slot(UN)][:, :], in_offset=None,
                        out_offset=bass.IndirectOffsetOnAxis(ap=ids[t.slot(UN)][:, :], axis=0),
                    ).then_inc(s_os[l][t.slot(UN)], 16)
                pipeline(pool, NT, UN, 0, tile)
                for r in range(UN):
                    pool.wait_ge(s_os[l][r], 16 * NT // UN * (l + 1))

            for l in range(2):
                pipeline(pool, B, 8, 8, attention(l))
                end_phase(pool)
                pool.wait_ge(phase, 8 + 8 * l)
                scatter_tiles(l)
                end_phase(pool)
                pool.wait_ge(phase, 12 + 8 * l)


            def last(s):
                b = s.back(1)
                if live(b):
                    fmvd.wait(pool, b)
                    rsqrt(frp, b, rstd[b.slot(2)][:, 1:2], rstd[b.slot(2)][:, 0:1], mv[b.slot(2)][:, 1:2], mhalf[:, 0:1])
            pipeline(pool, B, 8, 3, last)

        @block.tensor
        def _(pe):
            link = linker(pe, "pe")

            def mm(out_, lhsT, rhs, start=True, stop=True):
                return pe.matmul(out_, lhsT, rhs, start=start, stop=stop)

            def tr(out_, in_, n, idn=ident):
                return pe.transpose(out_, in_, idn[0:n, 0:n])

            def set_up(l):
                if l == 0:
                    hear(pe, "ident")
                    pe.wait_ge(ld["w0"], 16 * 6)
                    pe.wait_ge(ld["ctx"], 16)
                    tr(bank[0][:, 0:P], w_nat[:, 0, :], P)
                    tr(bank[0][0:C, P:2 * P], wkv_nat[:, 0, :], P)
                    link(tr(bank[0][0:C, 2 * P:3 * P], wkv_nat[:, 1, :], P))
                    tell(pe, "wT0")
                    for b in range(B):
                        ins = tr(bank[2 + b // 6][0:C, b % 6 * KL:(b % 6 + 1) * KL], ctx_nat[:, b, :], KL)
                    link(ins)
                    tell(pe, "ctxT")
                else:
                    hear(pe, "free1")
                    pe.wait_ge(ld["w1"], 16 * len(LATE))
                    tr(bank[0][:, 0:E], wr_nat[:, :], E)
                    link(tr(bank[0][:, P:2 * P], w_nat[:, 3, :], P))
                    tell(pe, "wT1")
                hear(pe, f"w{l}")
                hear(pe, f"perm{l}")
                for j in range(2):
                    ins = tr(bank[1][:, j * P:(j + 1) * P], wo_perm[:, j * P:(j + 1) * P], P)
                link(ins)
                tell(pe, f"woT{l}")
                if l == 0:
                    hear(pe, "ctxS")
                for g in range(3):
                    n = min(6, B - 6 * g) * KL
                    ins = mm(bank[5 + g][:, 0:n], wk[l][:, :], ctxT[:, 6 * g * KL:6 * g * KL + n])
                link(ins)
                tell(pe, f"k{l}")
                hear(pe, f"woS{l}")
                for b in range(B):
                    ins = mm(bank[1 + b // 4][0:KL, b % 4 * D:(b % 4 + 1) * D], ctxT[:, b * KL:(b + 1) * KL], wv[l][:, :])
                link(ins)
                tell(pe, f"v{l}")

            def attention(l):
                S = layers[l]

                def scores_for_max(b, u):
                    if u == 0:
                        s_qd[l].wait(pe, b)
                        s_kd[l].wait(pe, b)
                    bk = bank[(3 * b.c + u) % 2]
                    S["mx"].wait(pe, b, u - 1)
                    h0, h1 = SM_UNITS[u]
                    for h in range(h0, h1):
                        ins = mm(bk[:, (h - h0) * KL:(h - h0 + 1) * KL], q_st[b.slot(UN)][0:MAXROW, h, :],
                                 k_st[b.slot(UN)][0:MAXROW, h, :])
                    ins.then_inc(S["sm"].sem, 1)

                def scores(b, u):
                    if u == 0:
                        s_md[l].wait(pe, b)
                    bk = bank[2 + u % 2]
                    S["ex"].wait(pe, b, u - 1)
                    for i in range(4):
                        ins = mm(bk[0:KL, i * T:(i + 1) * T], k_st[b.slot(UN)][:, 4 * u + i, :],
                                 q_st[b.slot(UN)][:, 4 * u + i, :])
                    ins.then_inc(S["st"].sem, 1)

                def values(b, u):
                    if u == 0:
                        S["vx"].wait(pe, b)
                        S["od"].wait(pe, b.back(1))
                    S["ex"].wait(pe, b, u + 1)
                    c0 = 0 if u < 3 else T
                    for i in range(4):
                        ins = mm(bank[4][32 * i:32 * i + 32, c0:c0 + T], v_x[b.slot(2)][:, 4 * u + i, :],
                                 probs[u][:, i, :], start=u in (0, 3), stop=u in (2, 3))
                    ins.then_inc(S["pv"].sem, 1)

                def step(s):
                    b1, b3, b4, b5, b7, b8 = (s.back(n) for n in (1, 3, 4, 5, 7, 8))
                    if live(b1):
                        S["xn"].wait(pe, b1)
                        S["mtc"].wait(pe, b1.back(3))
                        tr(bank[6][:, 0:P], xn[b1.slot(2)][:, :], P).then_inc(S["t1"].sem, 1)
                    if live(b3):
                        scores_for_max(b3, 0)
                        scores_for_max(b3, 1)
                    if live_pair(b7):
                        S["f2"].wait(pe, b7)
                        S["f4"].wait(pe, b7.back(2), 1)
                        for j in range(2):
                            ins = tr(bank[7][:, j * P:(j + 1) * P], xfp[b7.c // 2 % 2][:, j, 0:D], P)
                        ins.then_inc(S["t2"].sem, 1)
                    if live(b5):
                        S["od"].wait(pe, b5)
                        S["x2"].wait(pe, b5.back(1))
                        mm(bank[5][:, 0:T], sel[:, 0:P], od[:, 0:T])
                        mm(bank[5][:, T:2 * T], sel[:, P:2 * P], od[:, T:2 * T]).then_inc(S["bc"].sem, 1)
                    if live(b1):
                        S["c1"].wait(pe, b1)
                        mm(bank[6][:, P:2 * P], wq[l][:, :], xnT[:, :]).then_inc(S["q"].sem, 1)
                    if live(b3):
                        scores_for_max(b3, 2)
                    if live(b4):
                        scores(b4, 0)
                        scores(b4, 1)
                    if live_pair(b7):
                        S["c2"].wait(pe, b7)
                        for j in range(2):
                            ins = mm(bank[7][:, 256 + E * j:256 + E * (j + 1)], xfT[:, j * P:(j + 1) * P], gate[l][:, :])
                        ins.then_inc(S["lg"].sem, 1)
                    if live(b4):
                        values(b4, 0)
                        scores(b4, 2)
                    if live(b3):
                        S["mp"].wait(pe, b3)
                        S["qs"].wait(pe, b1 if live(b1) else Step(B - 1))
                        tr(bank[6][0:2 * H, 2 * P:2 * P + P // 2].bitcast(BF16),
                           mxp[b3.slot(2)][:, :, :].rearrange("p s h -> p (s h)"), P, identb).then_inc(S["mt"].sem, 1)
                    if live(b4):
                        values(b4, 1)
                        scores(b4, 3)
                        values(b4, 2)
                        values(b4, 3)
                    if live_pair(b8):
                        S["f3"].wait(pe, b8, 8)
                        r0, r1 = bank[7][:, 272:280], bank[7][:, 280:288]
                        mm(r0, tri[:, :], mb[:, 0, :], True, False)
                        mm(r0, onesb[:, :], cum[:, :], False, True)
                        mm(r1, tri[:, :], mb[:, 1, :], True, False)
                        mm(r1, onesb[:, :], mb[:, 0, :], False, False)
                        mm(r1, onesb[:, :], cum[:, :], False, True).then_inc(S["rk"].sem, 1)
                    if live(b5):
                        S["ro"].wait(pe, b5)
                        mm(bank[5][:, 2 * T:3 * T], on[:, 0:T], wo[l][:, 0:D], True, False)
                        mm(bank[5][:, 2 * T:3 * T], on[:, T:2 * T], wo[l][:, D:2 * D], False, True)\
                            .then_inc(S["wo"].sem, 1)
                return step

            def experts(l):
                S = layers[l]
                e_reg = [pe.alloc_register(f"expert{l}_{k}") for k in range(UN)]

                def load_expert(t):
                    apart(pe)
                    pe.reg_load(e_reg[t.slot(UN)], r_exp[0:1, bass.ds(t.at(1), 1)])

                def expert_of(t):
                    return pe.snap(e_reg[t.slot(UN)], min_val=0, max_val=(E - 1) * F)

                def step(s):
                    t1, t2, t3 = s.back(1), s.back(2), s.back(3)
                    if tile_live(t1):
                        S["xtc"].wait(pe, t1)
                        S["act"].wait(pe, t1.back(2))
                        bk, e1 = bank[1 + t1.slot(2)], expert_of(t1)
                        if l == 1:
                            mm(bk[:, :], onesb[0:3, :], b1r[:, bass.ds(e1, F)], True, False)
                        mm(bk[:, :], xgT[t1.slot(2)][:, :], wa1[:, bass.ds(e1, F)], l == 0, True).then_inc(S["m1"].sem, 1)
                    if tile_live(s):
                        s_xg[l].wait(pe, s)
                        S["xtc"].wait(pe, s.back(1))
                        tr(bank[0][:, 0:P], xg[s.slot(UN)][:, 0:D], P).then_inc(S["xt"].sem, 1)
                        load_expert(s)
                    if tile_live(t2):
                        S["act"].wait(pe, t2)
                        S["htc"].wait(pe, t2.back(2))
                        for c in range(FC):
                            ins = tr(bank[3 + t2.slot(2)][:, c * P:(c + 1) * P], hid[t2.slot(2)][:, c * P:(c + 1) * P], P)
                        ins.then_inc(S["ht"].sem, 1)
                    if tile_live(t3):
                        S["htc"].wait(pe, t3)
                        S["oc"].wait(pe, t3.back(2))
                        bk, e3 = bank[5 + t3.slot(2)], expert_of(t3)
                        if l == 1:
                            mm(bk[:, 0:D], onesb[0:3, :], b2r[:, bass.ds(e3, D)], True, False)
                        for c in range(FC):
                            ins = mm(bk[:, 0:D], hidT[t3.slot(2)][:, c * P:(c + 1) * P],
                                     wa2[:, bass.ds(e3 + c * D, D)], l == 0 and c == 0, c == FC - 1)
                        ins.then_inc(S["m2"].sem, 1)
                return step

            set_up(0)
            end_phase(pe)
            pe.wait_ge(phase, 4)
            for l in range(2):
                S = layers[l]
                pipeline(pe, B, 8, 8, attention(l))
                S["f4"].wait(pe, Step(B - 1), 7)
                link(mm(bank[7][:, 0:E], onesb[:, :], cum[:, :]))
                tell(pe, f"count{l}")
                if l == 0:
                    set_up(1)
                    pe.wait_ge(ld["wa1"], 16)
                    pe.wait_ge(ld["wa2"], 16)
                else:
                    pe.wait_ge(ld["wb1"], 16)
                    pe.wait_ge(ld["wb2"], 16)
                    for g in range(2 * E):
                        src = (wb1 if g < E else wb2)[:, g % E * F:(g % E + 1) * F]
                        if g >= 4:
                            pe.wait_ge(w_copied, g - 3)
                        for c in range(FC):
                            ins = tr(bank[g % 4][:, c * P:(c + 1) * P], src[:, c * P:(c + 1) * P], P)
                        ins.then_inc(w_turned, 1)
                end_phase(pe)
                pe.wait_ge(phase, 8 + 8 * l)
                if l == 1:
                    pe.wait_ge(ld["bias"], 16 * 6)
                pipeline(pe, NT, 8, 3, experts(l))
                end_phase(pe)
                pe.wait_ge(phase, 12 + 8 * l)

        @block.scalar
        def _(act):
            link = linker(act, "act")

            def copy(out_, in_):
                return act.activation(out_, in_, ACT.Copy)

            def set_up(l):
                if l == 0:
                    act.wait_ge(ld["w0"], 16 * 6)
                    link(act.activation(tg[:, :], g_in[:, :], ACT.Tanh))
                    tell(act, "tg")
                    hear(act, "ctxT")
                    for g in range(3):
                        n = min(6, B - 6 * g) * KL
                        link(copy(ctxT[:, 6 * g * KL:6 * g * KL + n], bank[2 + g][0:C, 0:n]))
                    tell(act, "ctxS")
                hear(act, f"woT{l}")
                link(copy(wo[l][:, :], bank[1][:, 0:2 * P]))
                tell(act, f"woS{l}")
                hear(act, f"v{l}")
                for g in range(4):
                    link(copy(v_all[:, 4 * g * D:4 * (g + 1) * D], bank[1 + g][0:KL, :]))
                if l == 1:
                    tell(act, "v_raw1")

            def attention(l):
                S = layers[l]

                def exps(b, u):
                    S["st"].wait(act, b, u + 1)
                    S["pv"].wait(act, b.back(1), u + 1)
                    act.activation(probs[u][:, :, :].rearrange("p i q -> p (i q)"), bank[2 + u % 2][0:KL, :], ACT.Exp)\
                        .then_inc(S["ex"].sem, 1)

                def step(s):
                    b1, b3, b4, b7, b8 = (s.back(n) for n in (1, 3, 4, 7, 8))
                    if live(b1):
                        S["t1"].wait(act, b1)
                        S["q"].wait(act, b1.back(1))
                        copy(xnT[:, :], bank[6][:, 0:P]).then_inc(S["c1"].sem, 1)
                    if live(b1):
                        S["q"].wait(act, b1)
                        S["qp"].wait(act, b1.back(1))
                        b = b1.back(2)
                        s_qd[l].wait(act, b)
                        for dst in (q_f[:, :], q_p[b1.slot(2)][:, 0, :]):
                            if l == 0:
                                ins = act.activation(dst, bank[6][:, P:2 * P], ACT.Copy, scale=SCALE)
                            else:
                                ins = act.activation(dst, bank[6][:, P:2 * P], ACT.Identity, scale=SCALE, bias=bqs[:, :])
                            ins.then_inc(S["qs"].sem, 1)
                    if live_pair(b7):
                        S["t2"].wait(act, b7)
                        S["lg"].wait(act, b7.back(2))
                        copy(xfT[:, :], bank[7][:, 0:2 * P]).then_inc(S["c2"].sem, 1)
                    if live(b4):
                        exps(b4, 0)
                        exps(b4, 1)
                    if live(b3):
                        S["mt"].wait(act, b3)
                        b = b3.back(2)
                        s_md[l].wait(act, b)
                        copy(mxT[b3.slot(2)][:, :], bank[6][0:2 * H, 2 * P:2 * P + P // 2].bitcast(BF16))\
                            .then_inc(S["mtc"].sem, 1)
                    if live(b4):
                        exps(b4, 2)
                        exps(b4, 3)
                    if live(b4):
                        S["pv"].wait(act, b4)
                        S["ro"].wait(act, b4.back(1))
                        copy(od[:, :], bank[4][:, 0:2 * T]).then_inc(S["od"].sem, 1)
                    if live_pair(b8):
                        S["f3"].wait(act, b8, 9)
                        act.activation(gexp[:, :], gap[:, :], ACT.Exp).then_inc(S["ew"].sem, 1)
                return step

            def experts(l):
                S = layers[l]
                func = ACT.Gelu_apprx_tanh if l == 0 else ACT.Relu

                def step(s):
                    t = s.back(1)
                    if tile_live(t):
                        S["m1"].wait(act, t)
                        S["ht"].wait(act, t.back(2))
                        act.activation(hid[t.slot(2)][:, :], bank[1 + t.slot(2)][:, :], func).then_inc(S["act"].sem, 1)
                    if tile_live(s):
                        S["xt"].wait(act, s)
                        S["m1"].wait(act, s.back(2))
                        copy(xgT[s.slot(2)][:, :], bank[0][:, 0:P]).then_inc(S["xtc"].sem, 1)
                return step

            set_up(0)
            end_phase(act)
            act.wait_ge(phase, 4)
            for l in range(2):
                pipeline(act, B, 8, 8, attention(l))
                if l == 0:
                    set_up(1)
                else:
                    for g in range(2 * E):
                        act.wait_ge(w_turned, g + 1)
                        dst = (wa1 if g < E else wa2)[:, g % E * F:(g % E + 1) * F]
                        copy(dst, bank[g % 4][:, :]).then_inc(w_copied, 1)
                end_phase(act)
                act.wait_ge(phase, 8 + 8 * l)
                pipeline(act, NT, 8, 3, experts(l))
                end_phase(act)
                act.wait_ge(phase, 12 + 8 * l)

        @block.vector
        def _(_dve):
            dve = nc.vector
            link = linker(dve, "dve")

            def bc3(ap, n):
                return ap.unsqueeze(1).to_broadcast([P, n, ap.shape[1]])

            def inner(ap, n):
                return ap.unsqueeze(2).to_broadcast([P, ap.shape[1], n])

            def dh(ap):
                return ap.rearrange("p (h d) -> p d h", d=HD)

            def as_dh(ap):
                return ap.rearrange("p (d h) -> p d h", d=HD)

            def split3(out_, f, r):
                link(dve.tensor_copy(out_[:, 0, :], f))
                link(dve.tensor_tensor(r, f, out_[:, 0, :], ALU.subtract))
                link(dve.tensor_copy(out_[:, 1, :], r))
                link(dve.tensor_tensor(out_[:, 2, :], r, out_[:, 1, :], ALU.subtract))

            def set_up(l):
                hear(dve, f"wT{l}")
                if l == 0:
                    link(dve.tensor_copy(as_dh(wk[0][:, :]), dh(bank[0][0:C, P:2 * P])))
                    link(dve.tensor_copy(as_dh(wq[0][:, :]), dh(bank[0][:, 0:P])))
                    link(dve.tensor_copy(wv[0][:, :], bank[0][0:C, 2 * P:3 * P]))
                    w_o = w_nat[:, 1, :]
                else:
                    link(dve.tensor_copy(as_dh(wk[1][:, :]), dh(wk1_nat[:, :])))
                    link(dve.tensor_copy(as_dh(wq[1][:, :]), dh(w_nat[:, 2, :])))
                    link(dve.tensor_copy(gate[1][:, :], bank[0][:, 0:E]))
                    link(dve.tensor_scalar(bqs[:, :], bqk[:, 0:1], SCALE, None, ALU.mult))
                    w_o = bank[0][:, P:2 * P]
                tell(dve, f"w{l}")
                link(dve.memset(wo_perm[:, :], 0.0))
                link(dve.tensor_copy(
                    wo_perm[:, 0:P].rearrange("p (i j d) -> p j i d", i=4, j=4)[:, 0:3],
                    w_o.rearrange("p (j i d) -> p j i d", j=4, i=4)[:, 0:3]))
                link(dve.tensor_copy(
                    wo_perm[:, P:2 * P].rearrange("p (i r) -> p i r", i=4)[:, :, 0:HD],
                    w_o.rearrange("p (j i d) -> p j i d", j=4, i=4)[:, 3]))
                tell(dve, f"perm{l}")
                hear(dve, f"k{l}")
                for g in range(3):
                    n = min(6, B - 6 * g) * KL
                    cols = slice(6 * g * KL, 6 * g * KL + n)
                    if l == 0:
                        link(dve.tensor_copy(k_f[:, cols], bank[5 + g][:, 0:n]))
                    else:
                        link(dve.tensor_scalar(k_f[:, cols], bank[5 + g][:, 0:n], bqk[:, 1:2], None, ALU.add))
                split3(k_p, k_f, k_res[:, :])
                tell(dve, f"kparts{l}")
                if l == 1:
                    hear(dve, "v_raw1")
                    va = v_all[:, :].rearrange("p (b d) -> p b d", b=B)
                    link(dve.tensor_tensor(va, va, bv[:, :].unsqueeze(1).to_broadcast([KL, B, D]), ALU.add))
                    split3(b1_p, b1_in[:, :], b1_res[:, :])
                    split3(b2_p, b2_in[:, :], b2_res[:, :])
                    link(dve.tensor_scalar(bo[:, :], bo[:, :], tg[:, 1:2], None, ALU.mult))
                    link(dve.tensor_scalar(gam[:, :], gam[:, :], tg[:, 3:4], None, ALU.mult))
                    link(dve.tensor_scalar(bet[:, :], bet[:, :], tg[:, 3:4], None, ALU.mult))

            def norm_stats(stage_, b, src, st_, mv_, k0):
                apart(dve)
                dve.bn_stats(st_, src).then_inc(stage_.sem, 1)
                stage_.wait(dve, b, k0 + 1)
                apart(dve)
                dve.bn_aggr(mv_, st_).then_inc(stage_.sem, 1)

            def attention(l):
                S = layers[l]

                def step(s):
                    b1, b3, b5, b6, b8 = (s.back(n) for n in (1, 3, 5, 6, 8))
                    if live(b1):
                        S["rs1"].wait(dve, b1)
                        S["t1"].wait(dve, b1.back(2))
                        r = b1.slot(2)
                        dve.tensor_scalar(xn[r][:, :], x[:, seq(b1)], mv[r][:, 0:1], rstd[r][:, 1:2],
                                          ALU.subtract, ALU.mult).then_inc(S["xn"].sem, 1)
                    if live(b6):
                        S["wo"].wait(dve, b6)
                        if l == 1:
                            S["xb"].wait(dve, b6)
                        dve.scalar_tensor_tensor(x[:, seq(b6)], bank[5][:, 2 * T:3 * T], tg[:, l:l + 1], x[:, seq(b6)],
                                                 ALU.mult, ALU.add).then_inc(S["x2"].sem, 1)
                    if live(b3):
                        r = b3.slot(2)
                        S["mt"].wait(dve, b3.back(2))
                        for u, (h0, h1) in enumerate(SM_UNITS):
                            S["sm"].wait(dve, b3, u + 1)
                            n = h1 - h0
                            dve.tensor_reduce(mx[r][:, h0:h1],
                                              bank[(3 * b3.c + u) % 2][:, 0:n * KL].rearrange("p (h k) -> p h k", h=n),
                                              AX.X, ALU.max).then_inc(S["mx"].sem, 1)
                        S["mx"].wait(dve, b3)
                        dve.tensor_copy(mxp[r][:, 0, :], mx[r][:, :]).then_inc(S["mp"].sem, 1)
                        S["mp"].wait(dve, b3, 1)
                        dve.tensor_tensor(mxp[r][:, 1, :], mx[r][:, :], mxp[r][:, 0, :], ALU.subtract)\
                            .then_inc(S["mp"].sem, 1)
                    if live_pair(b6):
                        f1 = S["f1"]
                        S["x2"].wait(dve, b6)
                        S["rs2"].wait(dve, b6.back(2))
                        apart(dve)
                        for j in range(2):
                            dve.bn_stats(fstats[:, j, :], x[:, seq(b6.back(1 - j))]).then_inc(f1.sem, 1)
                        for j in range(2):
                            f1.wait(dve, b6, j + 1)
                            apart(dve)
                            dve.bn_aggr(fmv[:, j, :], fstats[:, j, :]).then_inc(f1.sem, 1)
                    if live(b1):
                        S["qs"].wait(dve, b1)
                        r = b1.slot(2)
                        qp = S["qp"]
                        dve.tensor_tensor(q_res[:, :], q_f[:, :], q_p[r][:, 0, :], ALU.subtract).then_inc(qp.sem, 1)
                        qp.wait(dve, b1, 1)
                        dve.tensor_copy(q_p[r][:, 1, :], q_res[:, :]).then_inc(qp.sem, 1)
                        qp.wait(dve, b1, 2)
                        dve.tensor_tensor(q_p[r][:, 2, :], q_res[:, :], q_p[r][:, 1, :], ALU.subtract)\
                            .then_inc(qp.sem, 1)
                    if live(b5):
                        S["bc"].wait(dve, b5)
                        dve.reciprocal(rec[:, :], bank[5][:, 0:2 * T]).then_inc(S["ro"].sem, 1)
                        S["ro"].wait(dve, b5, 1)
                        S["wo"].wait(dve, b5.back(1))
                        dve.tensor_tensor(on[:, :], od[:, :], rec[:, :], ALU.mult).then_inc(S["ro"].sem, 1)
                    if live_pair(b8):
                        f3 = S["f3"]
                        S["lg"].wait(dve, b8)
                        raw = bank[7][:, 256:256 + 2 * E].rearrange("p (j e) -> p j e", j=2)
                        if l == 0:
                            dve.tensor_copy(lg[:, :, :], raw).then_inc(f3.sem, 1)
                        else:
                            dve.tensor_tensor(lg[:, :, :], raw, bc3(br[:, :], 2), ALU.add).then_inc(f3.sem, 1)
                        f3.wait(dve, b8, 1)
                        apart(dve)
                        for j in range(2):
                            dve.max(top[:, j, :], lg[:, j, :]).then_inc(f3.sem, 1)
                        f3.wait(dve, b8, 3)
                        apart(dve)
                        for j in range(2):
                            dve.max_index(topi[:, j, :], top[:, j, :], lg[:, j, :]).then_inc(f3.sem, 1)
                        f3.wait(dve, b8, 5)
                        dve.tensor_copy(ei[:, :, :], topi[:, :, 0:2]).then_inc(f3.sem, 1)
                        f3.wait(dve, b8, 6)
                        dve.tensor_tensor(oh[:, :, :], bc3(iota8[:, :], 4),
                                          inner(ei[:, :, :].rearrange("p j k -> p (j k)"), E), ALU.is_equal)\
                            .then_inc(f3.sem, 1)
                        f3.wait(dve, b8, 7)
                        ohv = oh[:, :, :].rearrange("p (j k) e -> p j k e", k=2)
                        dve.tensor_tensor(mb[:, :, :], ohv[:, :, 0, :], ohv[:, :, 1, :], ALU.add).then_inc(f3.sem, 1)
                        dve.tensor_tensor(gap[:, :], top[:, :, 1], top[:, :, 0], ALU.subtract).then_inc(f3.sem, 1)
                    if l == 1 and live(s):
                        cm = S["cmb"]
                        s_ob[0].wait(dve, s)
                        for k in range(2):
                            if k:
                                cm.wait(dve, s, 1)
                            dve.scalar_tensor_tensor(x[:, seq(s)], ob[s.slot(UN)][:, k, :],
                                                     w01g[:, bass.ds(s.at(2, k), 1)], x[:, seq(s)],
                                                     ALU.mult, ALU.add).then_inc(cm.sem, 1)
                        cm.wait(dve, s, 2)
                    if live(s):
                        if l == 0 and s.i is None and s.c in (0, 4, 6, 7):
                            dve.wait_ge(ld[f"x{(0, 4, 6, 7).index(s.c)}"], 16)
                        S["rs1"].wait(dve, s.back(2))
                        norm_stats(S["ln1"], s, x[:, seq(s)], stats[s.slot(2)][:, :], mv[s.slot(2)][:, :], 0)
                    if live_pair(b6):
                        r = b6.c // 2 % 2
                        S["rs2"].wait(dve, b6)
                        b = b6.back(4)
                        if b.i is not None or b.c >= 0:
                            dve.wait_ge(s_sc[r], b.lap(4, 64, 128 + l * SC_LAYER))
                        for j in range(2):
                            dve.tensor_scalar(xfp[r][:, j, 0:D], x[:, seq(b6.back(1 - j))], fmv[:, j, 0:1], frs[:, j, 1:2],
                                              ALU.subtract, ALU.mult).then_inc(S["f2"].sem, 1)
                    if live_pair(b8):
                        f4, r = S["f4"], b8.c // 2 % 2
                        S["rk"].wait(dve, b8)
                        dve.tensor_tensor(rk[:, :, :], bank[7][:, 272:288].rearrange("p (j e) -> p j e", j=2),
                                          bc3(regoff[:, :], 2), ALU.add).then_inc(f4.sem, 1)
                        f4.wait(dve, b8, 1)
                        dve.tensor_tensor(pick[:, :, :].rearrange("p (j k) e -> p k j e", k=2),
                                          oh[:, :, :].rearrange("p (j k) e -> p k j e", k=2),
                                          rk[:, :, :].unsqueeze(1).to_broadcast([P, 2, 2, E]), ALU.mult)\
                            .then_inc(f4.sem, 1)
                        f4.wait(dve, b8, 2)
                        with nc.allow_low_precision(reason="row numbers, exact in float32 and int32"):
                            dve.tensor_reduce(slots[r][:, :], pick[:, :, :], AX.X, ALU.add).then_inc(f4.sem, 1)
                        dve.tensor_copy(xfp[r][:, :, D + 1], ei[:, :, 0]).then_inc(f4.sem, 1)
                        dve.tensor_copy(xfp[r][:, :, D], tok[:, bass.ds(b8.at(1, -1), 2)]).then_inc(f4.sem, 1)
                        dve.tensor_tensor(cum[:, :], cum[:, :], mb[:, 0, :], ALU.add).then_inc(f4.sem, 1)
                        f4.wait(dve, b8, 6)
                        dve.tensor_tensor(cum[:, :], cum[:, :], mb[:, 1, :], ALU.add).then_inc(f4.sem, 1)
                        S["ew"].wait(dve, b8)
                        dve.tensor_scalar(gden[:, :], gexp[:, :], 1.0, None, ALU.add).then_inc(f4.sem, 1)
                        f4.wait(dve, b8, 8)
                        wv_ = w01[:, bass.ds(b8.at(2, -2), 4)].rearrange("p (j k) -> p j k", j=2)
                        dve.reciprocal(wv_[:, :, 0], gden[:, :]).then_inc(f4.sem, 1)
                        f4.wait(dve, b8, 9)
                        dve.tensor_tensor(wv_[:, :, 1], wv_[:, :, 0], gexp[:, :], ALU.mult).then_inc(f4.sem, 1)
                return step

            def route(l):
                tt, ts = dve.tensor_tensor, dve.tensor_scalar

                def total(out_, in_):
                    link(dve.tensor_reduce(out_, in_, AX.X, ALU.add))

                hear(dve, f"count{l}")
                link(dve.tensor_copy(nE[:, :], bank[7][:, 0:E]))
                link(tt(cmp16[:, :, :], inner(nE[:, :], B), bc3(iota16[:, :], E), ALU.is_gt))
                total(tE[:, :], cmp16[:, :, :])
                link(tt(cmp8[:, :, :], bc3(tE[:, :], E), lt8[:, :, :], ALU.mult))
                total(cE[:, :], cmp8[:, :, :])
                link(tt(fE[:, :], cE[:, :], tE[:, :], ALU.subtract))
                link(tt(t8a[:, :, :], inner(iotat[:, :], E), bc3(cE[:, :], NT), ALU.is_ge))
                total(t_e[:, :], t8a[:, :, :])
                link(tt(t8a[:, :, :], bc3(iota8[:, :], NT), inner(t_e[:, :], E), ALU.is_equal))
                link(tt(t8b[:, :, :], t8a[:, :, :], bc3(nE[:, :], NT), ALU.mult))
                total(t_n[:, :], t8b[:, :, :])
                link(tt(t8b[:, :, :], t8a[:, :, :], bc3(fE[:, :], NT), ALU.mult))
                total(t_f[:, :], t8b[:, :, :])
                link(tt(t_j[:, :], iotat[:, :], t_f[:, :], ALU.subtract))
                link(ts(t_j[:, :], t_j[:, :], float(P), None, ALU.mult))
                link(ts(t_n[:, :], t_n[:, :], float(-P), None, ALU.add))
                link(tt(t_rel[:, :], t_j[:, :], t_n[:, :], ALU.min))
                link(ts(t_ec[:, :], t_e[:, :], float(E - 1), None, ALU.min))
                link(dve.scalar_tensor_tensor(t_row[:, :], t_ec[:, :], float(REGION), t_rel[:, :], ALU.mult, ALU.add))
                link(ts(r_row[:, :], t_row[:, :], float(P), None, ALU.add))
                link(ts(r_exp[:, :], t_ec[:, :], float(F), None, ALU.mult))
                link(dve.scalar_tensor_tensor(t_valid[:, :], t_rel[:, :], iotap[:, :], t_j[:, :], ALU.add, ALU.is_ge))
                link(tt(t_alt[:, :], t_valid[:, :], altbase[:, :], ALU.mult))
                link(tt(t_alt[:, :], altbase[:, :], t_alt[:, :], ALU.subtract))
                tell(dve, f"tiles{l}")

            def experts(l):
                S = layers[l]

                def step(s):
                    t = s.back(2)
                    if tile_live(t):
                        S["ht"].wait(dve, t)
                        S["m2"].wait(dve, t.back(2))
                        dve.tensor_copy(hidT[t.slot(2)][:, :], bank[3 + t.slot(2)][:, :]).then_inc(S["htc"].sem, 1)
                    if tile_live(t):
                        r, idt = t.slot(UN), S["id"]
                        s_xg[l].wait(dve, t)
                        b = t.back(UN)
                        s_os[l].wait(dve, b)
                        one = bass.ds(t.at(1), 1)
                        dve.tensor_scalar(idf[:, 0:1], xg[r][:, D + 1:D + 2], t_e[:, one], float(NTOK),
                                          ALU.not_equal, ALU.mult).then_inc(idt.sem, 1)
                        idt.wait(dve, t, 1)
                        dve.tensor_tensor(idf[:, 1:2], idf[:, 0:1], xg[r][:, D:D + 1], ALU.add).then_inc(idt.sem, 1)
                        idt.wait(dve, t, 2)
                        dve.tensor_scalar(ids[r][:, :], idf[:, 1:2], t_valid[:, one], t_alt[:, one],
                                          ALU.mult, ALU.add).then_inc(idt.sem, 1)
                    t = s.back(3)
                    if tile_live(t):
                        S["m2"].wait(dve, t)
                        b = t.back(UN)
                        s_os[l].wait(dve, b)
                        dve.tensor_copy(o_sb[t.slot(UN)][:, :], bank[5 + t.slot(2)][:, 0:D]).then_inc(S["oc"].sem, 1)
                return step

            set_up(0)
            end_phase(dve)
            dve.wait_ge(phase, 4)
            for l in range(2):
                link(dve.memset(cum[:, :], 0.0))
                if l == 1:
                    hear(dve, "tg")
                    link(dve.tensor_scalar(w01g[:, :], w01[:, :], tg[:, 2:3], None, ALU.mult))
                pipeline(dve, B, 8, 8, attention(l))
                S = layers[l]
                S["f4"].wait(dve, Step(B - 1))
                S["x2"].wait(dve, Step(B - 1))
                if l == 0:
                    tell(dve, "free1")
                route(l)
                if l == 0:
                    set_up(1)
                end_phase(dve)
                dve.wait_ge(phase, 8 + 8 * l)
                pipeline(dve, NT, 8, 3, experts(l))
                if l == 1:
                    xv = x[:, :].rearrange("p (b d) -> p b d", b=B)
                    link(dve.tensor_tensor(xv, xv, bet[:, :].unsqueeze(1).to_broadcast([P, B, D]), ALU.add))
                end_phase(dve)
                dve.wait_ge(phase, 12 + 8 * l)

            def last(s):
                b = s.back(2)
                if live(b):
                    m, r = mix[b.slot(UN)], b.slot(2)
                    frp.wait(dve, b)
                    q = b.back(UN)
                    s_store.wait(dve, q)
                    dve.tensor_scalar(m[:, :], m[:, :], mv[r][:, 0:1], rstd[r][:, 1:2], ALU.subtract, ALU.mult)\
                        .then_inc(fb.sem, 1)
                    fb.wait(dve, b, 1)
                    dve.tensor_tensor(m[:, :], m[:, :], gam[:, :], ALU.mult).then_inc(fb.sem, 1)
                    fb.wait(dve, b, 2)
                    dve.tensor_tensor(res[b.slot(UN)][:, :], m[:, :], x[:, seq(b)], ALU.add).then_inc(fb.sem, 1)
                if live(s):
                    m = mix[s.slot(UN)]
                    s_ob[1].wait(dve, s)
                    fb.wait(dve, s.back(UN))
                    dve.scalar_tensor_tensor(m[:, :], ob[s.slot(UN)][:, 0, :], w01[:, bass.ds(s.at(2), 1)],
                                             tgt[:, seq(s)], ALU.mult, ALU.add).then_inc(fa.sem, 1)
                    fa.wait(dve, s, 1)
                    dve.scalar_tensor_tensor(m[:, :], ob[s.slot(UN)][:, 1, :], w01[:, bass.ds(s.at(2, 1), 1)],
                                             m[:, :], ALU.mult, ALU.add).then_inc(fa.sem, 1)
                    fa.wait(dve, s, 2)
                    frp.wait(dve, s.back(2))
                    apart(dve)
                    dve.bn_stats(stats[s.slot(2)][:, :], m[:, :]).then_inc(fa.sem, 1)
                    fa.wait(dve, s, 3)
                    apart(dve)
                    dve.bn_aggr(mv[s.slot(2)][:, :], stats[s.slot(2)][:, :]).then_inc(fmvd.sem, 1)
            pipeline(dve, B, 8, 3, last)


NAMES = ["x", "ctx_512", "g_xattn", "g_ffn", "L0_xattn_Wq", "L0_xattn_Wkv", "L0_xattn_Wo", "L0_ffn_gate_w", "L0_ffn_w1",
         "L0_ffn_w2", "L1_xattn_Wq", "L1_xattn_bq", "L1_xattn_Wk", "L1_xattn_bk", "L1_xattn_Wv", "L1_xattn_bv",
         "L1_xattn_Wo", "L1_xattn_bo", "L1_ffn_Wr", "L1_ffn_br", "L1_ffn_W1", "L1_ffn_b1", "L1_ffn_W2", "L1_ffn_b2",
         "L1_ffn_gamma", "L1_ffn_beta"]


def kernel(**inputs):
    import numpy as _np
    import concourse.bacc as _bacc
    from concourse import mybir as _mybir
    from concourse.bass_utils import run_bass_kernel_spmd as _run

    nc = _bacc.Bacc("TRN2", target_bir_lowering=False, num_devices=1)
    arrays, args = {}, {}
    for name in NAMES:
        v = _np.ascontiguousarray(inputs[name])
        arrays[f"in_{name}"] = v
        args[name] = nc.dram_tensor(f"in_{name}", v.shape, _mybir.dt.from_np(v.dtype), kind="ExternalInput").ap()
    out = nc.dram_tensor("out_0", (B, T, D), _mybir.dt.float32, kind="ExternalOutput").ap()
    build(nc, args, out)
    r = _run(nc, [arrays], core_ids=[0])
    return r.results[0]["out_0"]
```
